# Optimizing a Trainium2 kernel written in Bass

```python
import numpy as np
import jax
import jax.numpy as jnp

def _softmax(x, axis=-1):
    return jax.nn.softmax(x, axis=axis)

def _gelu(x):
    return jax.nn.gelu(x, approximate=True)

def _silu(x):
    return jax.nn.silu(x)

def _sigmoid(x):
    return jax.nn.sigmoid(x)

def _layernorm(x, axis=-1, eps=1e-05):
    m = jnp.mean(x, axis=axis, keepdims=True)
    v = jnp.var(x, axis=axis, keepdims=True)
    return (x - m) / jnp.sqrt(v + eps)

def _scatter_add(tgt, idx, src, axis=0):
    return tgt.at[idx].add(src)

def _segment_sum(src, seg, n):
    return jax.ops.segment_sum(src, seg, n)
kernel_name = 'mk_seq_postln_d1_jaxref_r8_f2b1ae'

def setup_inputs(seed: int=0):
    np.random.seed(seed)
    _w = jnp.asarray

    def _L0_attn_setup():
        import jax, jax.numpy as jnp
        import numpy as np
        D_MODEL = 512
        D_XB = 128
        D_INNER = 512
        HEADDIM = 128
        DSTATE = 128
        NHEADS = D_INNER // HEADDIM
        DCONV = 4
        INTER = 1792
        EPS = 1e-05
        CHUNK = 128

        def rmsnorm(x, w):
            return x * jax.lax.rsqrt(jnp.mean(x * x, axis=-1, keepdims=True) + EPS) * w

        def silu(x):
            return x * jax.nn.sigmoid(x)

        def mamba2(x, w_in, conv_w, conv_b, A_log, D, dt_bias, w_out):
            B, L, _ = x.shape
            H, P, N = (NHEADS, HEADDIM, DSTATE)
            G = D_XB // P
            rep = H // G
            zxbcdt = x @ w_in.T
            z, xs, Bs, Cs, dt = jnp.split(zxbcdt, [D_INNER, D_INNER + D_XB, D_INNER + 2 * D_XB, 2 * D_INNER + 2 * D_XB], axis=-1)
            xBC = jnp.concatenate([xs, Bs, Cs], axis=-1)
            conv = jax.lax.conv_general_dilated(xBC.transpose(0, 2, 1), conv_w[:, None, :], (1,), [(DCONV - 1, 0)], feature_group_count=conv_w.shape[0])
            xBC = silu(conv.transpose(0, 2, 1) + conv_b)
            xs, Bs, Cs = jnp.split(xBC, [D_XB, 2 * D_XB], axis=-1)
            dt = jax.nn.softplus(dt + dt_bias)
            A = -jnp.exp(A_log)
            xh = jnp.repeat(xs.reshape(B, L, G, P), rep, axis=2)
            Bh = jnp.repeat(Bs.reshape(B, L, G, N), rep, axis=2)
            Ch = Cs.reshape(B, L, H, N)
            c, Q = (L // CHUNK, CHUNK)
            a = (dt * A).reshape(B, c, Q, H).transpose(0, 1, 3, 2)
            dtc = dt.reshape(B, c, Q, H).transpose(0, 1, 3, 2)
            Xc = xh.reshape(B, c, Q, H, P).transpose(0, 1, 3, 2, 4)
            Bc = Bh.reshape(B, c, Q, H, N).transpose(0, 1, 3, 2, 4)
            Cc = Ch.reshape(B, c, Q, H, N).transpose(0, 1, 3, 2, 4)
            cs = jnp.cumsum(a, axis=-1)
            tri = jnp.tril(jnp.ones((Q, Q), bool))
            Ldec = jnp.where(tri, jnp.exp(cs[..., :, None] - cs[..., None, :]), 0.0)
            Xdt = Xc * dtc[..., None]
            att = jnp.einsum('bchqn,bchkn->bchqk', Cc, Bc) * Ldec
            Yd = jnp.einsum('bchqk,bchkp->bchqp', att, Xdt)
            dec_end = jnp.exp(cs[..., -1:] - cs)
            states = jnp.einsum('bchq,bchqn,bchqp->bchpn', dec_end, Bc, Xdt)
            g = jnp.exp(cs[..., -1])

            def step(S, inp):
                gk, st = inp
                return (gk[:, :, None, None] * S + st, S)
            S0 = jnp.zeros((B, H, P, N), x.dtype)
            _, prev = jax.lax.scan(step, S0, (g.transpose(1, 0, 2), states.transpose(1, 0, 2, 3, 4)))
            prev = prev.transpose(1, 0, 2, 3, 4)
            Yo = jnp.einsum('bchqn,bchpn,bchq->bchqp', Cc, prev, jnp.exp(cs))
            Y = (Yd + Yo).transpose(0, 1, 3, 2, 4).reshape(B, L, H, P)
            Y = Y + D[:, None] * xh
            y = Y.reshape(B, L, D_INNER) * silu(z)
            return y @ w_out.T
        key = jax.random.key(seed)
        ks = jax.random.split(key, 10)
        B, L = (2, 256)
        proj_out = 2 * D_INNER + 2 * D_XB + NHEADS
        conv_dim = 2 * D_XB + D_INNER
        return {'hidden_states': jax.random.normal(ks[0], (B, L, D_MODEL), jnp.float32), 'w_in': jax.random.normal(ks[1], (proj_out, D_MODEL), jnp.float32) * 0.02, 'conv_w': jax.random.normal(ks[2], (conv_dim, DCONV), jnp.float32) * 0.1, 'conv_b': jnp.zeros((conv_dim,), jnp.float32), 'A_log': jnp.log(jnp.arange(1, NHEADS + 1, dtype=jnp.float32)), 'D': jnp.ones((NHEADS,), jnp.float32), 'dt_bias': jax.random.normal(ks[3], (NHEADS,), jnp.float32) * 0.1, 'w_out': jax.random.normal(ks[4], (D_MODEL, D_INNER), jnp.float32) * 0.02, 'ln1_w': jnp.ones((D_MODEL,), jnp.float32), 'ln2_w': jnp.ones((D_MODEL,), jnp.float32), 'gate_w': jax.random.normal(ks[5], (INTER, D_MODEL), jnp.float32) * 0.02, 'up_w': jax.random.normal(ks[6], (INTER, D_MODEL), jnp.float32) * 0.02, 'down_w': jax.random.normal(ks[7], (D_MODEL, INTER), jnp.float32) * 0.02}
    _L0_attn_in = _L0_attn_setup()

    def _L0_ffn_setup():
        import jax, jax.numpy as jnp
        import numpy as np
        EPS = 1e-05

        def _bitlinear(x, w):
            scale = jnp.mean(jnp.abs(w))
            q = jnp.round(jnp.clip(w / (scale + EPS), -1.0, 1.0))
            deq = q * scale
            return x @ deq.T
        key = jax.random.key(seed)
        k1, k2, k3, k4 = jax.random.split(key, 4)
        B, S, H, I = (4, 256, 512, 1376)
        return {'hidden_states': jax.random.normal(k1, (B, S, H), dtype=jnp.float32), 'w_gate': jax.random.normal(k2, (I, H), dtype=jnp.float32) * 0.02, 'w_up': jax.random.normal(k3, (I, H), dtype=jnp.float32) * 0.02, 'w_down': jax.random.normal(k4, (H, I), dtype=jnp.float32) * 0.02}
    _L0_ffn_in = _L0_ffn_setup()
    _d = {'L0_attn_hidden_states': _L0_attn_in['hidden_states'], 'L0_attn_w_in': _L0_attn_in['w_in'], 'L0_attn_conv_w': _L0_attn_in['conv_w'], 'L0_attn_conv_b': _L0_attn_in['conv_b'], 'L0_attn_A_log': _L0_attn_in['A_log'], 'L0_attn_D': _L0_attn_in['D'], 'L0_attn_dt_bias': _L0_attn_in['dt_bias'], 'L0_attn_w_out': _L0_attn_in['w_out'], 'L0_attn_ln1_w': _L0_attn_in['ln1_w'], 'L0_attn_ln2_w': _L0_attn_in['ln2_w'], 'L0_attn_gate_w': _L0_attn_in['gate_w'], 'L0_attn_up_w': _L0_attn_in['up_w'], 'L0_attn_down_w': _L0_attn_in['down_w'], 'L0_ffn_w_gate': _L0_ffn_in['w_gate'], 'L0_ffn_w_up': _L0_ffn_in['w_up'], 'L0_ffn_w_down': _L0_ffn_in['w_down']}
    _x0 = _d['L0_attn_hidden_states']
    _d['L0_attn_hidden_states'] = jax.random.normal(jax.random.fold_in(jax.random.key(seed), 1), (2, 512, 512), dtype=_x0.dtype)
    del _x0
    return _d

def reference(L0_attn_hidden_states, L0_attn_w_in, L0_attn_conv_w, L0_attn_conv_b, L0_attn_A_log, L0_attn_D, L0_attn_dt_bias, L0_attn_w_out, L0_attn_ln1_w, L0_attn_ln2_w, L0_attn_gate_w, L0_attn_up_w, L0_attn_down_w, L0_ffn_w_gate, L0_ffn_w_up, L0_ffn_w_down):

    def _L0_attn_ref(hidden_states, w_in, conv_w, conv_b, A_log, D, dt_bias, w_out, ln1_w, ln2_w, gate_w, up_w, down_w):
        import jax, jax.numpy as jnp
        import numpy as np
        D_MODEL = 512
        D_XB = 128
        D_INNER = 512
        HEADDIM = 128
        DSTATE = 128
        NHEADS = D_INNER // HEADDIM
        DCONV = 4
        INTER = 1792
        EPS = 1e-05
        CHUNK = 128

        def rmsnorm(x, w):
            return x * jax.lax.rsqrt(jnp.mean(x * x, axis=-1, keepdims=True) + EPS) * w

        def silu(x):
            return x * jax.nn.sigmoid(x)

        def mamba2(x, w_in, conv_w, conv_b, A_log, D, dt_bias, w_out):
            B, L, _ = x.shape
            H, P, N = (NHEADS, HEADDIM, DSTATE)
            G = D_XB // P
            rep = H // G
            zxbcdt = x @ w_in.T
            z, xs, Bs, Cs, dt = jnp.split(zxbcdt, [D_INNER, D_INNER + D_XB, D_INNER + 2 * D_XB, 2 * D_INNER + 2 * D_XB], axis=-1)
            xBC = jnp.concatenate([xs, Bs, Cs], axis=-1)
            conv = jax.lax.conv_general_dilated(xBC.transpose(0, 2, 1), conv_w[:, None, :], (1,), [(DCONV - 1, 0)], feature_group_count=conv_w.shape[0])
            xBC = silu(conv.transpose(0, 2, 1) + conv_b)
            xs, Bs, Cs = jnp.split(xBC, [D_XB, 2 * D_XB], axis=-1)
            dt = jax.nn.softplus(dt + dt_bias)
            A = -jnp.exp(A_log)
            xh = jnp.repeat(xs.reshape(B, L, G, P), rep, axis=2)
            Bh = jnp.repeat(Bs.reshape(B, L, G, N), rep, axis=2)
            Ch = Cs.reshape(B, L, H, N)
            c, Q = (L // CHUNK, CHUNK)
            a = (dt * A).reshape(B, c, Q, H).transpose(0, 1, 3, 2)
            dtc = dt.reshape(B, c, Q, H).transpose(0, 1, 3, 2)
            Xc = xh.reshape(B, c, Q, H, P).transpose(0, 1, 3, 2, 4)
            Bc = Bh.reshape(B, c, Q, H, N).transpose(0, 1, 3, 2, 4)
            Cc = Ch.reshape(B, c, Q, H, N).transpose(0, 1, 3, 2, 4)
            cs = jnp.cumsum(a, axis=-1)
            tri = jnp.tril(jnp.ones((Q, Q), bool))
            Ldec = jnp.where(tri, jnp.exp(cs[..., :, None] - cs[..., None, :]), 0.0)
            Xdt = Xc * dtc[..., None]
            att = jnp.einsum('bchqn,bchkn->bchqk', Cc, Bc) * Ldec
            Yd = jnp.einsum('bchqk,bchkp->bchqp', att, Xdt)
            dec_end = jnp.exp(cs[..., -1:] - cs)
            states = jnp.einsum('bchq,bchqn,bchqp->bchpn', dec_end, Bc, Xdt)
            g = jnp.exp(cs[..., -1])

            def step(S, inp):
                gk, st = inp
                return (gk[:, :, None, None] * S + st, S)
            S0 = jnp.zeros((B, H, P, N), x.dtype)
            _, prev = jax.lax.scan(step, S0, (g.transpose(1, 0, 2), states.transpose(1, 0, 2, 3, 4)))
            prev = prev.transpose(1, 0, 2, 3, 4)
            Yo = jnp.einsum('bchqn,bchpn,bchq->bchqp', Cc, prev, jnp.exp(cs))
            Y = (Yd + Yo).transpose(0, 1, 3, 2, 4).reshape(B, L, H, P)
            Y = Y + D[:, None] * xh
            y = Y.reshape(B, L, D_INNER) * silu(z)
            return y @ w_out.T
        res = hidden_states
        h = rmsnorm(hidden_states, ln1_w)
        h = res + mamba2(h, w_in, conv_w, conv_b, A_log, D, dt_bias, w_out)
        res = h
        h2 = rmsnorm(h, ln2_w)
        mlp = silu(h2 @ gate_w.T) * (h2 @ up_w.T) @ down_w.T
        return res + mlp

    def _L0_ffn_ref(hidden_states, w_gate, w_up, w_down):
        import jax, jax.numpy as jnp
        import numpy as np
        EPS = 1e-05

        def _bitlinear(x, w):
            scale = jnp.mean(jnp.abs(w))
            q = jnp.round(jnp.clip(w / (scale + EPS), -1.0, 1.0))
            deq = q * scale
            return x @ deq.T
        gate = _bitlinear(hidden_states, w_gate)
        up = _bitlinear(hidden_states, w_up)
        inter = gate * up
        out = _bitlinear(inter, w_down)
        return out
    x = L0_attn_hidden_states
    x = _layernorm(x + _L0_attn_ref(x, L0_attn_w_in, L0_attn_conv_w, L0_attn_conv_b, L0_attn_A_log, L0_attn_D, L0_attn_dt_bias, L0_attn_w_out, L0_attn_ln1_w, L0_attn_ln2_w, L0_attn_gate_w, L0_attn_up_w, L0_attn_down_w), axis=-1)
    x = _layernorm(x + _L0_ffn_ref(x, L0_ffn_w_gate, L0_ffn_w_up, L0_ffn_w_down), axis=-1)
    return x

_drawn_inputs = setup_inputs


def setup_inputs(seed=0):
    import zlib

    import numpy as np

    out = dict(_drawn_inputs(seed))
    spreads = {'L0_attn_conv_b': (0.0, 0.8),
     'L0_attn_D': (1.0, 0.6),
     'L0_attn_ln1_w': (1.0, 0.6),
     'L0_attn_ln2_w': (1.0, 0.6)}
    factors = {'L0_attn_w_in': 8.0,
     'L0_attn_conv_w': 8.0,
     'L0_attn_A_log': 8.0,
     'L0_attn_dt_bias': 8.0,
     'L0_attn_w_out': 7.365,
     'L0_attn_gate_w': 64.0,
     'L0_attn_up_w': 64.0,
     'L0_attn_down_w': 64.0}
    for name, (base, spread) in spreads.items():
        noise = np.random.default_rng([zlib.crc32(name.encode()), seed]).standard_normal(out[name].shape)
        drawn = base * np.exp(spread * noise) if base else spread * noise
        out[name] = jnp.asarray(drawn.astype(out[name].dtype))
    for name, factor in factors.items():
        out[name] = (out[name] * factor).astype(out[name].dtype)
    return out
```

```python
from contextlib import ExitStack

import numpy as np
import concourse.bass as bass
from concourse import mybir

F32 = mybir.dt.float32
F32R = mybir.dt.float32r
BF16 = mybir.dt.bfloat16
ALU = mybir.AluOpType
ACT = mybir.ActivationFunctionType

P = 128
NB, L, D = 2, 512, 512
KD = D // P
NC = L // P
NT = NB * NC
H = 4
NX = 2 + H
NZ = H
TAPS = 4
FM = 1792 // P
I = 1376
FF = -(-I // P)
NIN = (NX + NZ) // 2
EPS = 1e-5
RAW = 2 * KD * P
MASKED = -3.0e38


def build_schedule():
    steps, loads = [], []

    def load(kind, *which):
        loads.append((kind, *which))
        return ("load", len(loads) - 1)

    def scan_round(b, r):
        now = []
        if r < NC:
            now.append(("chunk", b, r))
        if 0 <= r - 1 < NC:
            now.append(("state", b, r - 1))
        if 0 <= r - 2 < NC:
            now.append(("norm2", b, r - 2))
        if r < NC:
            now.append(("decay", b, r))
        if 0 <= r - 1 < NC:
            now.append(("outproj", b, r - 1))
        if 0 <= r - 2 < NC:
            now.append(("turn2", b, r - 2))
        return now

    steps += [("norm1", 0), load("in", 0), ("norm1", 1), ("turn1", 0), ("norm1", 2), ("turn1", 1),
              ("norm1", 3), ("turn1", 2), ("turn1", 3), ("dt", 0)]
    later = [("norm1", 4), ("norm1", 5), ("turn1", 4), ("norm1", 6), ("turn1", 5), ("norm1", 7),
             ("turn1", 6), ("turn1", 7)]
    for j in range(NX + NZ):
        if j % 2 == 0 and j // 2 + 1 < NIN:
            steps.append(load("in", j // 2 + 1))
        steps.append(("inproj", 0, j))
        if j >= 1 and later:
            steps.append(later.pop(0))
    steps += later + [load("out", 0), load("out", 1)]
    steps.append(("dt", 1))
    steps += scan_round(0, 0)
    rounds = [scan_round(0, 1), scan_round(0, 2), scan_round(0, 3)]
    for j in range(NX + NZ):
        steps.append(("inproj", 1, j))
        if j % 3 == 1 and rounds:
            steps += rounds.pop(0)
    steps += [load("gu", 0, 0)]
    steps += scan_round(0, 4) + scan_round(1, 0) + scan_round(0, 5) + scan_round(1, 1)
    rounds = [scan_round(1, r) for r in range(2, 6)]
    sums = [("sumgu", f) for f in range(FF)] + [("sumdn", p) for p in range(FF // 2 + 1)]
    for f in range(FM):
        steps.append(load("gu", 0, f + 1) if f + 1 < FM else load("dn", 0, 0))
        steps.append(("gateup", 0, f))
        if f % 2 == 1 and rounds:
            steps += rounds.pop(0)
        if f >= 1:
            steps.append(load(*sums.pop(0)))
    steps.append(("act", 0, 0))
    for f in range(FM):
        if f % 2 == 0:
            steps.append(load("dn", 0, f // 2 + 1) if f // 2 + 1 < FM // 2 else load("gu", 1, 0))
        if f + 1 < FM:
            steps.append(("act", 0, f + 1))
        steps.append(("down", 0, f))
        if sums and f % 2 == 1:
            steps.append(load(*sums.pop(0)))
    tern = [("qgu", f) for f in range(FF)] + [("qdn", p) for p in range(FF // 2 + 1)]
    between = [("ln1", 0), ("ln1", 1), ("ln1x", 0), ("ln1", 2), ("ln1x", 1), ("ln1t", 0), ("ln1", 3), ("ln1x", 2),
               ("ln1t", 1), ("ln1x", 3), ("ln1t", 2), ("ln1t", 3)]
    for f in range(FM):
        steps.append(load("gu", 1, f + 1) if f + 1 < FM else load("dn", 1, 0))
        steps.append(("gateup", 1, f))
        if f == 0:
            steps += between[:4] + [("scales",)]
            between = between[4:]
        elif between:
            steps += between[:3]
            between = between[3:]
        if f >= 2:
            steps.append(load(*tern.pop(0)))
    steps.append(("act", 1, 0))
    for f in range(FM):
        if f % 2 == 0 and f // 2 + 1 < FM // 2:
            steps.append(load("dn", 1, f // 2 + 1))
        if f + 1 < FM:
            steps.append(("act", 1, f + 1))
        steps.append(("down", 1, f))
        if tern and f % 2 == 1:
            steps.append(load(*tern.pop(0)))
    between = [("ln1", 4), ("ln1", 5), ("ln1x", 4), ("ln1", 6), ("ln1x", 5), ("ln1t", 4), ("ln1", 7), ("ln1x", 6),
               ("ln1t", 5), ("ln1x", 7), ("ln1t", 6), ("ln1t", 7)]
    for b in range(NB):
        for f in range(FF):
            steps.append(("ffn", b, f))
            if b == 0:
                steps += between[:3]
                between = between[3:]
            if f >= 1:
                steps.append(("inter", b, f - 1))
        steps.append(("inter", b, FF - 1))
        for c in range(NC):
            steps.append(("ffndown", b, c))
            if c >= 1:
                steps.append(("ln2", b, c - 1))
        steps.append(("ln2", b, NC - 1))
    assert not (sums or tern or between or rounds)
    return steps, loads


SCHEDULE, LOADS = build_schedule()
RAW_SLOTS = 2
SPLITS = [n for n, w in enumerate(LOADS) if w[0] in ("in", "out", "gu", "dn")]
STREAMED = [n for n in SPLITS if LOADS[n][0] in ("gu", "dn")]


def psum_jobs():
    a, b = [], []
    for s in SCHEDULE:
        kind, at = s[0], s[1:]
        if kind == "dt":
            a.append(("dt", *at))
            b.append(("cs", *at))
        elif kind == "inproj":
            a.append(("in", *at))
        elif kind == "gateup":
            a += [("g", *at), ("u", *at)]
        elif kind == "ffn":
            a += [("fg", *at), ("fu", *at)]
        elif kind in ("turn1", "ln1t", "scales"):
            b.append((kind, *at))
        elif kind == "chunk":
            b += [("xb", *at), ("csb", *at), ("cb", *at)]
        elif kind == "state":
            b += ([("st", *at)] if at[1] < NC - 1 else []) + [("y", *at)]
        elif kind in ("outproj", "turn2", "ffndown"):
            b.append((kind, *at))
        elif kind == "down" and at[1] == 0:
            b += [("down", at[0], c) for c in range(NC)]
    return {j: n for n, j in enumerate(a)}, {j: n for n, j in enumerate(b)}


JOB_A, JOB_B = psum_jobs()


def layer_kernel(nc, hidden, w_in, w_dt, conv_w, conv_b, a_log, d_skip, dt_bias, w_out, ln1_w, ln2_w,
                 w_gu, w_dn, f_gu, f_dn, out):
    with ExitStack() as ctx:
        def sb(name, shape, dt=F32, scope=ctx):
            return scope.enter_context(nc.sbuf_tensor(name, shape, dt))

        def sem(name):
            return ctx.enter_context(nc.semaphore(name))

        x = sb("x", [P, NT, D])
        xT_h = sb("xT_h", [P, KD, NB * L], F32R)
        xT_l = sb("xT_l", [P, KD, NB * L], F32R)
        raw = sb("raw", [P, RAW_SLOTS, RAW])
        wst = sb("wst", [P, 2, 2, RAW], F32R)
        ident = sb("ident", [P, P])
        ones = sb("ones", [P, P])
        nrm = sb("nrm", [P, 2, D])
        junk = sb("junk", [P, D], BF16)
        wdt_raw = sb("wdt_raw", [P, KD * H])
        wdt_h = sb("wdt_h", [P, KD * H], F32R)
        wdt_l = sb("wdt_l", [P, KD * H], F32R)
        dskip_sb = sb("dskip_sb", [P, H])
        alog_sb = sb("alog_sb", [P, H])
        aneg = sb("aneg", [P, H])
        dtb_sb = sb("dtb_sb", [P, H])
        convw_sb = sb("convw_sb", [P, NX, TAPS])
        convb_sb = sb("convb_sb", [P, NX])
        minus_half = sb("minus_half", [P, 1])
        sq = sb("sq", [P, 2 * NT])
        var = sb("var", [P, 4 * NT])
        rstd = sb("rstd", [P, 4 * NT])
        bn6 = sb("bn6", [P, 2, 6])
        mv = sb("mv", [P, 2 * NT, 2])
        dtT = sb("dtT", [P, NB, NC * H])
        csT = sb("csT", [P, NB, NC * H])
        dtw = sb("dtw", [P, 8, NC * H])
        wend = sb("wend", [P, 2, H])
        gend = sb("gend", [P, 2, H])
        absum = sb("absum", [P, 3 * FF])
        scl = sb("scl", [P, 16])

        first = ExitStack()
        win_h = sb("win_h", [P, NIN, RAW], F32R, first)
        win_l = sb("win_l", [P, NIN, RAW], F32R, first)
        xbc0 = sb("xbc0", [P, NX, L], F32, first)
        sz0 = sb("sz0", [P, NZ, L], F32, first)
        first.close()
        mlp = ExitStack()
        act = sb("act", [P, FM, L], F32, mlp)
        act_hl = sb("act_hl", [P, 3, 2, L], F32R, mlp)
        silu_t = sb("silu_t", [P, 2, L], F32, mlp)
        qtmp = sb("qtmp", [P, RAW], BF16, mlp)
        mlp.close()
        ffn = ExitStack()
        int_h = sb("int_h", [P, FF, L], F32R, ffn)
        int_l = sb("int_l", [P, FF, L], F32R, ffn)
        gate_t = sb("gate_t", [P, 2, L], F32, ffn)
        prod_t = sb("prod_t", [P, 2, L], F32, ffn)
        ffn.close()
        keep1 = sb("region1", [P, NIN * RAW * 2 + (NX + NZ) * L])
        scan = ExitStack()
        xbc1 = sb("xbc1", [P, NX, L], F32, scan)
        sz1 = sb("sz1", [P, NZ, L], F32, scan)
        wout_h = sb("wout_h", [P, 2, RAW], F32R, scan)
        wout_l = sb("wout_l", [P, 2, RAW], F32R, scan)
        decay = sb("decay", [P, 2, H * P], F32, scan)
        ecs = sb("ecs", [P, 2, H * P], F32, scan)
        xnbn = sb("xnbn", [P, 2, 2 * P], F32, scan)
        xs = sb("xs", [P, H * P], F32, scan)
        state = sb("state", [P, 2, H * P], F32, scan)
        yt = sb("yt", [P, H * P], F32, scan)
        yt_h = sb("yt_h", [P, H * P], F32R, scan)
        yt_l = sb("yt_l", [P, H * P], F32R, scan)
        diag_d = sb("diag_d", [P, H * P], F32, scan)
        maskneg = sb("maskneg", [P, P], F32, scan)
        tri = sb("tri", [P, P], F32, scan)
        ln1_sb = sb("ln1_sb", [P, D], F32, scan)
        ln2_sb = sb("ln2_sb", [P, D], F32, scan)
        scan.close()
        q_gu = sb("q_gu", [P, FF, RAW], F32R)
        q_dn = sb("q_dn", [P, FF, D], F32R)
        xbc, sz = (xbc0, xbc1), (sz0, sz1)

        psA = ctx.enter_context(nc.psum_tensor("psA", [P, 4, 512], F32))
        psB = ctx.enter_context(nc.psum_tensor("psB", [P, 4, 512], F32))

        x_loaded = [sem(f"x_loaded{t}") for t in range(NT)]
        consts_loaded = sem("consts_loaded")
        raw_loaded = [sem(f"raw_loaded{i}") for i in range(RAW_SLOTS)]
        high_ready = sem("high_ready")
        low_ready = sem("low_ready")
        wdt_ready = sem("wdt_ready")
        consts_ready = sem("consts_ready")
        diag_ready = sem("diag_ready")
        a_done = sem("a_done")
        b_done = sem("b_done")
        a_free = [sem(f"a_free{i}") for i in range(4)]
        b_free = [sem(f"b_free{i}") for i in range(4)]
        sq_ready = sem("sq_ready")
        rstd_ready = sem("rstd_ready")
        nrm_ready = sem("nrm_ready")
        xTh_ready = sem("xTh_ready")
        aexp_ready = sem("aexp_ready")
        dte_in = sem("dte_in")
        dte_out = sem("dte_out")
        dtl_in = sem("dtl_in")
        dtl_out = sem("dtl_out")
        dt_ready = sem("dt_ready")
        conv_begun = sem("conv_begun")
        xbc_ready = sem("xbc_ready")
        expo_ready = sem("expo_ready")
        decay_ready = sem("decay_ready")
        gend_ready = sem("gend_ready")
        wend_ready = sem("wend_ready")
        xs_ready = sem("xs_ready")
        cs_scaled = sem("cs_scaled")
        yth_done = sem("yth_done")
        y_ready = sem("y_ready")
        u_ready = sem("u_ready")
        acth_ready = sem("acth_ready")
        actl_ready = sem("actl_ready")
        act_free = sem("act_free")
        sum_ready = sem("sum_ready")
        tern_ready = sem("tern_ready")
        bn_ready = sem("bn_ready")
        ln1_ready = sem("ln1_ready")
        inth_ready = sem("inth_ready")
        int_ready = sem("int_ready")
        out_ready = sem("out_ready")
        out_stored = sem("out_stored")
        dve_chain = sem("dve_chain")
        pool_chain = sem("pool_chain")

        def bank_a(job):
            return psA[:, JOB_A[job] % 4, :]

        def bank_b(job):
            return psB[:, JOB_B[job] % 4, :]

        def freed_a(job):
            return a_free[JOB_A[job] % 4], JOB_A[job] // 4 + 1

        def freed_b(job):
            return b_free[JOB_B[job] % 4], JOB_B[job] // 4 + 1


        def heads(tile):
            return tile.rearrange("p (h q) -> p h q", h=H)

        def chunk(c):
            return slice(c * P, (c + 1) * P)

        def load_number(*load):
            return LOADS.index(load)

        def split_count(*load):
            return SPLITS.index(load_number(*load)) + 1

        def wst_slot(*load):
            return STREAMED.index(load_number(*load)) % 2

        def raw_arrived(eng, n):
            eng.wait_ge(raw_loaded[n % RAW_SLOTS], 16 * (n // RAW_SLOTS + 1))

        def split_parts(n):
            kind, *at = LOADS[n]
            if kind == "in":
                return win_h[:, at[0], :], win_l[:, at[0], :]
            if kind == "out":
                return wout_h[:, at[0], :], wout_l[:, at[0], :]
            s = STREAMED.index(n) % 2
            return wst[:, s, 0, :], wst[:, s, 1, :]

        def exponents(b, c):
            return (expo_ready, (NC - 1) * b + c) if c else freed_b(("csb", b, c))

        def down_used(n):
            b, f = divmod(n, FM)
            if f == FM - 1:
                return b_done, JOB_B[("down", b, NC - 1)] + 1
            return act_free, (FM - 1) * b + f + 1

        def streamed_used(i):
            kind, b, f = LOADS[STREAMED[i]]
            return (a_done, JOB_A[("u", b, f)] + 1) if kind == "gu" else down_used(FM * b + 2 * f + 1)

        TERN = [n for n, w in enumerate(LOADS) if w[0] in ("qgu", "qdn")]
        SUMS = [n for n, w in enumerate(LOADS) if w[0] in ("sumgu", "sumdn")]
        TURNS = [s for s in SCHEDULE if s[0] in ("turn1", "turn2", "ln1t")]
        NORMS = [s for s in SCHEDULE if s[0] in ("norm1", "outproj", "ln1", "ln2")]
        CONSTS = 7
        N_CONST = 16 * (CONSTS + 1)

        def norm_number(step):
            return NORMS.index(step)

        def tile_of(step):
            return step[1] if len(step) == 2 else NC * step[1] + step[2]

        def job_of_turn(step):
            return step

        def raw_used(n):
            if n in SPLITS:
                return low_ready, SPLITS.index(n) + 1
            if n in TERN:
                return tern_ready, TERN.index(n) + 1
            return sum_ready, sum(sum_parts(m) for m in SUMS[:SUMS.index(n) + 1])

        def sum_parts(n):
            return 2 if LOADS[n][0] == "sumgu" else down_width(LOADS[n][1]) // D

        def down_width(p):
            return RAW if 2 * p + 1 < FF else D

        block = ctx.enter_context(nc.Block())

        @block.sync
        def _(sp):
            def load_x(t):
                sp.dma_start(x[:, t, :], hidden[t]).then_inc(x_loaded[t], 16)

            sources = {"in": w_in, "out": w_out, "sumgu": f_gu, "qgu": f_gu, "sumdn": f_dn, "qdn": f_dn}
            for t in range(2):
                load_x(t)
            for n, (kind, *at) in enumerate(LOADS):
                if n >= RAW_SLOTS:
                    sp.wait_ge(*raw_used(n - RAW_SLOTS))
                if kind in sources:
                    src = sources[kind][at[0]]
                else:
                    src = (w_gu if kind == "gu" else w_dn)[at[1]]
                wide = down_width(at[0]) if kind in ("sumdn", "qdn") else RAW
                sp.dma_start(raw[:, n % RAW_SLOTS, 0:wide], src[:, 0:wide]).then_inc(raw_loaded[n % RAW_SLOTS], 16)
                if n < 3:
                    load_x(2 * n + 2)
                    load_x(2 * n + 3)
            for t in range(NT):
                sp.wait_ge(out_ready, t + 1)
                sp.dma_start(out[t], x[:, t, :]).then_inc(out_stored, 16)
            sp.wait_ge(out_stored, 16 * NT)

        @block.gpsimd
        def _(pool):
            chain = [0]

            def link(ins):
                chain[0] += 1
                ins.then_inc(pool_chain, 1)
                pool.wait_ge(pool_chain, chain[0])

            def reciprocal_deviation(step, mean_square, factor):
                i = norm_number(step)
                link(nc.gpsimd.tensor_scalar(var[:, i:i + 1], mean_square, factor, EPS, ALU.mult, ALU.add))
                nc.gpsimd.tensor_tensor(rstd[:, i:i + 1], var[:, i:i + 1], minus_half[:], ALU.pow)\
                    .then_inc(rstd_ready, 1)

            nc.gpsimd.memset(minus_half[:], -0.5)
            nc.gpsimd.memset(ones[:], 1.0)
            nc.gpsimd.memset(ident[:], 0.0)
            nc.gpsimd.memset(tri[:], 1.0)
            link(nc.gpsimd.memset(maskneg[:], 0.0))
            nc.gpsimd.affine_select(out=ident[:], in_=ident[:], compare_op=ALU.not_equal, fill=1.0, base=0,
                                    pattern=[[-1, P]], channel_multiplier=1)
            nc.gpsimd.affine_select(out=tri[:], in_=tri[:], compare_op=ALU.is_ge, fill=0.0, base=0,
                                    pattern=[[1, P]], channel_multiplier=-1)
            nc.gpsimd.affine_select(out=maskneg[:], in_=maskneg[:], compare_op=ALU.is_ge, fill=MASKED, base=0,
                                    pattern=[[1, P]], channel_multiplier=-1).then_inc(consts_ready, 1)
            pool.wait_ge(consts_ready, 1)
            pool.wait_ge(consts_loaded, N_CONST)
            pool.wait_ge(wdt_ready, 1)
            nc.gpsimd.tensor_tensor(wdt_l[:], wdt_raw[:], wdt_h[:].bitcast(F32), ALU.subtract).then_inc(wdt_ready, 1)
            nc.gpsimd.tensor_tensor(heads(diag_d[:]), ident[:].unsqueeze(1).to_broadcast([P, H, P]),
                                    dskip_sb[:].unsqueeze(2).to_broadcast([P, H, P]), ALU.mult)\
                .then_inc(diag_ready, 1)

            for step in SCHEDULE:
                kind, at = step[0], step[1:]
                if kind == "load" and LOADS[at[0]][0] in ("in", "out", "gu", "dn"):
                    n = at[0]
                    high, low = split_parts(n)
                    pool.wait_ge(high_ready, SPLITS.index(n) + 1)
                    raw_arrived(pool, n)
                    if n in STREAMED and STREAMED.index(n) >= 2:
                        pool.wait_ge(*streamed_used(STREAMED.index(n) - 2))
                    nc.gpsimd.tensor_tensor(low, raw[:, n % RAW_SLOTS, :], high.bitcast(F32), ALU.subtract)\
                        .then_inc(low_ready, 1)
                elif kind == "norm1":
                    pool.wait_ge(sq_ready, at[0] + 1)
                    reciprocal_deviation(step, sq[:, at[0]:at[0] + 1], 1.0 / D)
                elif kind == "decay":
                    b, c = at
                    t = NC * b + c
                    if c < NC - 1:
                        i = (NC - 1) * b + c
                        pool.wait_ge(wend_ready, i + 1)
                        pool.wait_ge(*freed_b(("xb", b, c)))
                        if i >= 1:
                            before = (b, c - 1) if c else (b - 1, NC - 2)
                            pool.wait_ge(b_done, JOB_B[("st", *before)] + 1)
                        nc.gpsimd.tensor_tensor(heads(xs[:]), xnbn[:, t % 2, 0:P].unsqueeze(1).to_broadcast([P, H, P]),
                                                wend[:, t % 2, :].unsqueeze(2).to_broadcast([P, H, P]), ALU.mult)\
                            .then_inc(xs_ready, 1)
                    if c > 0:
                        i = (NC - 1) * b + c - 1
                        pool.wait_ge(*freed_b(("csb", b, c)))
                        pool.wait_ge(xbc_ready, NX * (b + 1))
                        nc.gpsimd.tensor_tensor(heads(ecs[:, t % 2, :]), heads(ecs[:, t % 2, :]),
                                                xbc[b][:, 2:NX, chunk(c)], ALU.mult).then_inc(cs_scaled, 1)
                elif kind == "outproj":
                    t = tile_of(step)
                    i = NT + t
                    pool.wait_ge(sq_ready, i + 1)
                    reciprocal_deviation(step, sq[:, i:i + 1], 1.0 / D)
                    pool.wait_ge(*freed_b(step))
                    nc.gpsimd.tensor_tensor(x[:, t, :], x[:, t, :], nrm[:, t % 2, :], ALU.add).then_inc(u_ready, 1)
                elif kind == "act":
                    b, f = at
                    n = FM * b + f
                    pool.wait_ge(acth_ready, n + 1)
                    nc.gpsimd.tensor_tensor(act_hl[:, n % 3, 1, :], act[:, f, :], act_hl[:, n % 3, 0, :].bitcast(F32),
                                            ALU.subtract).then_inc(actl_ready, 1)
                elif kind in ("ln1", "ln2"):
                    t = tile_of(step)
                    i = t if kind == "ln1" else NT + t
                    pool.wait_ge(bn_ready, i + 1)
                    reciprocal_deviation(step, mv[:, i, 1:2], 1.0)
                elif kind == "inter":
                    b, f = at
                    n = FF * b + f
                    pool.wait_ge(inth_ready, n + 1)
                    pool.wait_ge(*freed_a(("fu", b, f)))
                    nc.gpsimd.tensor_tensor(int_l[:, f, :], prod_t[:, n % 2, :], int_h[:, f, :].bitcast(F32),
                                            ALU.subtract).then_inc(int_ready, 1)

        @block.scalar
        def _(s):
            s.dma_start(wdt_raw[:], w_dt).then_inc(consts_loaded, 16)
            s.dma_start(ln1_sb[:], ln1_w.to_broadcast([P, D])).then_inc(consts_loaded, 16)
            s.dma_start(alog_sb[:], a_log.to_broadcast([P, H])).then_inc(consts_loaded, 16)
            s.dma_start(dtb_sb[:], dt_bias.to_broadcast([P, H])).then_inc(consts_loaded, 16)
            s.dma_start(dskip_sb[:], d_skip.to_broadcast([P, H])).then_inc(consts_loaded, 16)
            s.dma_start(convw_sb[:], conv_w).then_inc(consts_loaded, 16)
            s.dma_start(convb_sb[:], conv_b).then_inc(consts_loaded, 16)
            s.dma_start(ln2_sb[:], ln2_w.to_broadcast([P, D])).then_inc(consts_loaded, 16)
            s.wait_ge(consts_loaded, N_CONST)
            nc.scalar.activation(aneg[:], alog_sb[:], ACT.Exp).then_inc(aexp_ready, 1)
            nc.scalar.activation(wdt_h[:], wdt_raw[:], ACT.Copy).then_inc(wdt_ready, 1)

            def conv_silu(b, j):
                s.wait_ge(*freed_a(("in", b, j)))
                nc.scalar.activation(xbc[b][:, j, :], xbc[b][:, j, :], ACT.Silu).then_inc(xbc_ready, 1)

            sums = 0
            junk_written = []

            def sum_into(total, tile, func, ready):
                if junk_written:
                    s.wait_ge(*junk_written[-1])
                nc.scalar.activation(junk[:], tile, func, accum_out=total).then_inc(ready, 1)
                junk_written.append((ready, 1 + sum(r is ready for r, _ in junk_written)))

            for step in SCHEDULE:
                kind, at = step[0], step[1:]
                if kind == "load" and LOADS[at[0]][0] in ("in", "out", "gu", "dn"):
                    n = at[0]
                    high, _ = split_parts(n)
                    raw_arrived(s, n)
                    if n in STREAMED and STREAMED.index(n) >= 2:
                        s.wait_ge(*streamed_used(STREAMED.index(n) - 2))
                    nc.scalar.activation(high, raw[:, n % RAW_SLOTS, :], ACT.Copy).then_inc(high_ready, 1)
                elif kind == "load" and LOADS[at[0]][0] in ("sumgu", "sumdn"):
                    n = at[0]
                    what, f = LOADS[n]
                    raw_arrived(s, n)
                    if what == "sumgu":
                        parts = [(slice(0, RAW // 2), f), (slice(RAW // 2, RAW), FF + f)]
                    else:
                        wide = down_width(f)
                        parts = [(slice(k, k + D), None) for k in range(0, wide, D)]
                    for cols, col in parts:
                        if col is None:
                            col = 2 * FF + sums
                            sums += 1
                        sum_into(absum[:, col:col + 1], raw[:, n % RAW_SLOTS, cols], ACT.Abs, sum_ready)
                elif kind == "norm1":
                    t = at[0]
                    s.wait_ge(x_loaded[t], 16)
                    sum_into(sq[:, t:t + 1], x[:, t, :], ACT.Square, sq_ready)
                elif kind in ("turn1", "turn2", "ln1t"):
                    t = tile_of(step)
                    s.wait_ge(b_done, JOB_B[step] + 1)
                    nc.scalar.activation(xT_h[:, :, chunk(t)], bank_b(step).rearrange("p (k q) -> p k q", k=KD),
                                         ACT.Copy).then_inc(xTh_ready, 1)
                elif kind == "dt":
                    b = at[0]
                    s.wait_ge(dte_in, b + 1)
                    nc.scalar.activation(dtw[:, 2, :], dtw[:, 1, :], ACT.Exp).then_inc(dte_out, 1)
                    s.wait_ge(dtl_in, b + 1)
                    nc.scalar.activation(dtw[:, 4, :], dtw[:, 3, :], ACT.Ln).then_inc(dtl_out, 1)
                elif kind == "inproj":
                    b, j = at
                    job = ("in", b, j)
                    s.wait_ge(a_done, JOB_A[job] + 1)
                    if j < NX:
                        nc.scalar.activation(xbc[b][:, j, :], bank_a(job), ACT.Identity, bias=convb_sb[:, j:j + 1],
                                             scale=convw_sb[:, j, TAPS - 1:TAPS]).then_inc(conv_begun, 1)
                    else:
                        sem_free, _ = freed_a(job)
                        nc.scalar.activation(sz[b][:, j - NX, :], bank_a(job), ACT.Silu).then_inc(sem_free, 1)
                    if 1 <= j <= NX:
                        conv_silu(b, j - 1)
                elif kind == "chunk":
                    b, c = at
                    t = NC * b + c
                    s.wait_ge(b_done, JOB_B[("xb", b, c)] + 1)
                    if t >= 2:
                        s.wait_ge(b_done, JOB_B[("y", (t - 2) // NC, (t - 2) % NC)] + 1)
                    nc.scalar.activation(xnbn[:, t % 2, :], bank_b(("xb", b, c))[:, 0:2 * P], ACT.Copy)\
                        .then_inc(freed_b(("xb", b, c))[0], 1)
                    job = ("csb", b, c)
                    s.wait_ge(*exponents(b, c))
                    nc.scalar.activation(decay[:, t % 2, :], decay[:, t % 2, :], ACT.Exp).then_inc(decay_ready, 1)
                    if c > 0:
                        nc.scalar.activation(gend[:, t % 2, :], heads(bank_b(job))[:, :, P - 1], ACT.Exp)\
                            .then_inc(gend_ready, 1)
                        s.wait_ge(gend_ready, (NC - 1) * b + c)
                        nc.scalar.activation(ecs[:, t % 2, :], bank_b(job), ACT.Exp).then_inc(freed_b(job)[0], 1)
                elif kind == "state":
                    t = tile_of(step)
                    s.wait_ge(*freed_b(("y", *at)))
                    if t >= 1:
                        s.wait_ge(b_done, JOB_B[("outproj", (t - 1) // NC, (t - 1) % NC)] + 1)
                    nc.scalar.activation(yt_h[:], yt[:], ACT.Copy).then_inc(yth_done, 1)
                elif kind == "outproj":
                    t = tile_of(step)
                    s.wait_ge(*freed_b(step))
                    sum_into(sq[:, NT + t:NT + t + 1], nrm[:, t % 2, :], ACT.Square, sq_ready)
                elif kind == "gateup":
                    b, f = at
                    n = FM * b + f
                    job = ("g", b, f)
                    s.wait_ge(a_done, JOB_A[job] + 1)
                    if n >= 2:
                        s.wait_ge(*freed_a(("u", (n - 2) // FM, (n - 2) % FM)))
                    nc.scalar.activation(silu_t[:, n % 2, :], bank_a(job), ACT.Silu).then_inc(freed_a(job)[0], 1)
                elif kind == "act":
                    b, f = at
                    n = FM * b + f
                    s.wait_ge(*freed_a(("u", b, f)))
                    if n >= 3:
                        s.wait_ge(*down_used(n - 3))
                    nc.scalar.activation(act_hl[:, n % 3, 0, :], act[:, f, :], ACT.Copy).then_inc(acth_ready, 1)
                elif kind == "ffn":
                    b, f = at
                    n = FF * b + f
                    job = ("fg", b, f)
                    if n == 0:
                        s.wait_ge(tern_ready, len(TERN))
                    s.wait_ge(a_done, JOB_A[job] + 1)
                    if n >= 2:
                        s.wait_ge(*freed_a(("fu", (n - 2) // FF, (n - 2) % FF)))
                    nc.scalar.activation(gate_t[:, n % 2, :], bank_a(job), ACT.Copy).then_inc(freed_a(job)[0], 1)
                elif kind == "inter":
                    b, f = at
                    n = FF * b + f
                    s.wait_ge(*freed_a(("fu", b, f)))
                    nc.scalar.activation(int_h[:, f, :], prod_t[:, n % 2, :], ACT.Copy).then_inc(inth_ready, 1)

        @block.vector
        def _(v):
            chain = [0]

            def link(ins):
                chain[0] += 1
                ins.then_inc(dve_chain, 1)
                v.wait_ge(dve_chain, chain[0])

            def turned(step):
                n = TURNS.index(step)
                t = tile_of(step)
                v.wait_ge(xTh_ready, n + 1)
                nc.vector.tensor_tensor(xT_l[:, :, chunk(t)], bank_b(step).rearrange("p (k q) -> p k q", k=KD),
                                        xT_h[:, :, chunk(t)].bitcast(F32), ALU.subtract)\
                    .then_inc(freed_b(step)[0], 1)

            def statistics(t, i):
                link(nc.vector.bn_stats(bn6[:, i % 2, :], x[:, t, :]))
                nc.vector.bn_aggr(mv[:, i, :], bn6[:, i % 2, :]).then_inc(bn_ready, 1)

            for step in SCHEDULE:
                kind, at = step[0], step[1:]
                if kind == "norm1":
                    t = at[0]
                    v.wait_ge(rstd_ready, norm_number(step) + 1)
                    if t == 0:
                        v.wait_ge(consts_loaded, N_CONST)
                    v.wait_ge(x_loaded[t], 16)
                    if t >= 2:
                        v.wait_ge(b_done, JOB_B[("turn1", t - 2)] + 1)
                    nc.vector.scalar_tensor_tensor(out=nrm[:, t % 2, :], in0=x[:, t, :],
                                                   scalar=rstd[:, norm_number(step):norm_number(step) + 1],
                                                   in1=ln1_sb[:], op0=ALU.mult, op1=ALU.mult).then_inc(nrm_ready, 1)
                elif kind in ("turn1", "turn2", "ln1t"):
                    turned(step)
                elif kind == "dt":
                    b = at[0]
                    job = ("dt", b)
                    v.wait_ge(a_done, JOB_A[job] + 1)
                    v.wait_ge(aexp_ready, 1)
                    by_chunk = "p (c h) -> p c h"
                    chunks_heads = [P, NC, H]
                    nc.vector.tensor_tensor(dtw[:, 0, :].rearrange(by_chunk, h=H),
                                            bank_a(job)[:, 0:NC * H].rearrange(by_chunk, h=H),
                                            dtb_sb[:].unsqueeze(1).to_broadcast(chunks_heads), ALU.add)\
                        .then_inc(freed_a(job)[0], 1)
                    v.wait_ge(*freed_a(job))
                    nc.vector.scalar_tensor_tensor(out=dtw[:, 1, :], in0=dtw[:, 0, :], scalar=-1.0, in1=dtw[:, 0, :],
                                                   op0=ALU.mult, op1=ALU.min).then_inc(dte_in, 1)
                    v.wait_ge(dte_out, b + 1)
                    nc.vector.tensor_scalar(dtw[:, 3, :], dtw[:, 2, :], 1.0, None, ALU.add).then_inc(dtl_in, 1)
                    v.wait_ge(dtl_in, b + 1)
                    link(nc.vector.scalar_tensor_tensor(out=dtw[:, 5, :], in0=dtw[:, 3, :], scalar=-1.0,
                                                        in1=dtw[:, 2, :], op0=ALU.add, op1=ALU.subtract))
                    link(nc.vector.tensor_scalar(dtw[:, 6, :], dtw[:, 3, :], -0.5, 1.5, ALU.mult, ALU.add))
                    link(nc.vector.tensor_tensor(dtw[:, 5, :], dtw[:, 5, :], dtw[:, 6, :], ALU.mult))
                    v.wait_ge(dtl_out, b + 1)
                    link(nc.vector.tensor_tensor(dtw[:, 7, :], dtw[:, 4, :], dtw[:, 5, :], ALU.subtract))
                    link(nc.vector.scalar_tensor_tensor(out=dtT[:, b, :], in0=dtw[:, 0, :], scalar=0.0,
                                                        in1=dtw[:, 7, :], op0=ALU.max, op1=ALU.add))
                    link(nc.vector.tensor_scalar(dtw[:, 6, :], dtT[:, b, :], -1.0, None, ALU.mult))
                    if b > 0:
                        v.wait_ge(b_done, JOB_B[("cs", b - 1)] + 1)
                    nc.vector.tensor_tensor(dtw[:, 5, :].rearrange(by_chunk, h=H),
                                            dtw[:, 6, :].rearrange(by_chunk, h=H),
                                            aneg[:].unsqueeze(1).to_broadcast(chunks_heads), ALU.mult)\
                        .then_inc(dt_ready, 1)
                    job = ("cs", b)
                    v.wait_ge(b_done, JOB_B[job] + 1)
                    nc.vector.tensor_copy(csT[:, b, :], bank_b(job)[:, 0:NC * H]).then_inc(freed_b(job)[0], 1)
                elif kind == "inproj" and at[1] < NX:
                    b, j = at
                    job = ("in", b, j)
                    n = NX * b + j
                    v.wait_ge(conv_begun, n + 1)
                    for back in range(1, TAPS):
                        add = nc.vector.scalar_tensor_tensor(
                            out=xbc[b][:, j, back:L], in0=bank_a(job)[:, 0:L - back],
                            scalar=convw_sb[:, j, TAPS - 1 - back:TAPS - back], in1=xbc[b][:, j, back:L],
                            op0=ALU.mult, op1=ALU.add)
                        if back < TAPS - 1:
                            link(add)
                    add.then_inc(freed_a(job)[0], 1)
                elif kind == "chunk":
                    b, c = at
                    t = NC * b + c
                    job = ("csb", b, c)
                    v.wait_ge(b_done, JOB_B[job] + 1)
                    if c == 0:
                        v.wait_ge(*freed_b(("cs", b)))
                        v.wait_ge(consts_ready, 1)
                    if t >= 2:
                        v.wait_ge(b_done, JOB_B[("y", (t - 2) // NC, (t - 2) % NC)] + 1)
                    ready, _ = exponents(b, c)
                    for h in range(H):
                        expo = nc.vector.scalar_tensor_tensor(
                            out=decay[:, t % 2, chunk(h)], in0=bank_b(job)[:, chunk(h)],
                            scalar=csT[:, b, H * c + h:H * c + h + 1], in1=maskneg[:], op0=ALU.subtract, op1=ALU.min)
                    expo.then_inc(ready, 1)
                elif kind == "decay":
                    b, c = at
                    t = NC * b + c
                    v.wait_ge(decay_ready, t + 1)
                    if c < NC - 1:
                        i = (NC - 1) * b + c
                        if i >= 2:
                            v.wait_ge(xs_ready, i - 1)
                        nc.vector.tensor_tensor(wend[:, t % 2, :], heads(decay[:, t % 2, :])[:, :, P - 1],
                                                dtT[:, b, H * c:H * c + H], ALU.mult).then_inc(wend_ready, 1)
                        v.wait_ge(wend_ready, i + 1)
                    job = ("cb", b, c)
                    v.wait_ge(b_done, JOB_B[job] + 1)
                    for h in range(H):
                        att = nc.vector.scalar_tensor_tensor(
                            out=decay[:, t % 2, chunk(h)], in0=bank_b(job)[:, chunk(h)],
                            scalar=dtT[:, b, H * c + h:H * c + h + 1], in1=decay[:, t % 2, chunk(h)],
                            op0=ALU.mult, op1=ALU.mult)
                    att.then_inc(freed_b(job)[0], 1)
                elif kind == "state":
                    b, c = at
                    t = NC * b + c
                    job = ("y", b, c)
                    v.wait_ge(b_done, JOB_B[job] + 1)
                    v.wait_ge(*freed_a(("in", b, NX + NZ - 1)))
                    if t >= 1:
                        v.wait_ge(yth_done, t)
                    nc.vector.tensor_tensor(heads(yt[:]), heads(bank_b(job)), sz[b][:, :, chunk(c)], ALU.mult)\
                        .then_inc(freed_b(job)[0], 1)
                    if c < NC - 1:
                        job_s = ("st", b, c)
                        v.wait_ge(b_done, JOB_B[job_s] + 1)
                        if c == 0:
                            last = nc.vector.tensor_copy(state[:, 0, :], bank_b(job_s))
                        else:
                            v.wait_ge(gend_ready, (NC - 1) * b + c)
                            v.wait_ge(*freed_b(("st", b, c - 1)))
                            for h in range(H):
                                last = nc.vector.scalar_tensor_tensor(
                                    out=state[:, c % 2, chunk(h)], in0=state[:, (c - 1) % 2, chunk(h)],
                                    scalar=gend[:, t % 2, h:h + 1], in1=bank_b(job_s)[:, chunk(h)],
                                    op0=ALU.mult, op1=ALU.add)
                        last.then_inc(freed_b(job_s)[0], 1)
                    v.wait_ge(yth_done, t + 1)
                    nc.vector.tensor_tensor(yt_l[:], yt[:], yt_h[:].bitcast(F32), ALU.subtract).then_inc(y_ready, 1)
                elif kind == "outproj":
                    t = tile_of(step)
                    v.wait_ge(b_done, JOB_B[step] + 1)
                    before = ("turn1", NT - 2 + t) if t < 2 else ("turn2", (t - 2) // NC, (t - 2) % NC)
                    v.wait_ge(b_done, JOB_B[before] + 1)
                    nc.vector.tensor_tensor(nrm[:, t % 2, :], bank_b(step), x[:, t, :], ALU.add)\
                        .then_inc(freed_b(step)[0], 1)
                elif kind == "norm2":
                    t = tile_of(step)
                    i = norm_number(("outproj", *at))
                    v.wait_ge(rstd_ready, i + 1)
                    v.wait_ge(u_ready, t + 1)
                    nc.vector.scalar_tensor_tensor(out=nrm[:, t % 2, :], in0=nrm[:, t % 2, :], scalar=rstd[:, i:i + 1],
                                                   in1=ln2_sb[:], op0=ALU.mult, op1=ALU.mult).then_inc(nrm_ready, 1)
                elif kind == "gateup":
                    b, f = at
                    v.wait_ge(*freed_a(("g", b, f)))
                    job = ("u", b, f)
                    v.wait_ge(a_done, JOB_A[job] + 1)
                    nc.vector.tensor_tensor(act[:, f, :], silu_t[:, (FM * b + f) % 2, :], bank_a(job), ALU.mult)\
                        .then_inc(freed_a(job)[0], 1)
                elif kind == "scales":
                    v.wait_ge(b_done, JOB_B[step] + 1)
                    totals = bank_b(step)
                    edges = [0, FF, 2 * FF, 3 * FF]
                    for w in range(3):
                        nc.vector.tensor_reduce(scl[:, w:w + 1], totals[:, edges[w]:edges[w + 1]],
                                                mybir.AxisListType.X, ALU.add)\
                            .then_inc(dve_chain if w < 2 else freed_b(step)[0], 1)
                    chain[0] += 2
                    v.wait_ge(dve_chain, chain[0])
                    v.wait_ge(*freed_b(step))
                    link(nc.vector.tensor_scalar(scl[:, 3:6], scl[:, 0:3], 1.0 / (I * D), None, ALU.mult))
                    link(nc.vector.tensor_scalar(scl[:, 6:9], scl[:, 3:6], EPS, 0.5, ALU.add, ALU.mult))
                    link(nc.vector.tensor_scalar(scl[:, 9:12], scl[:, 6:9], -1.0, None, ALU.mult))
                    link(nc.vector.tensor_tensor(scl[:, 12:13], scl[:, 3:4], scl[:, 4:5], ALU.mult))
                    link(nc.vector.tensor_tensor(scl[:, 13:14], scl[:, 12:13], scl[:, 5:6], ALU.mult))
                elif kind == "load" and LOADS[at[0]][0] in ("qgu", "qdn"):
                    n = at[0]
                    what, f = LOADS[n]
                    raw_arrived(v, n)
                    if n == TERN[0]:
                        v.wait_ge(b_done, JOB_B[("turn2", NB - 1, NC - 1)] + 1)
                    if what == "qgu":
                        parts = [(slice(0, RAW // 2), 0, q_gu[:, f, 0:RAW // 2]),
                                 (slice(RAW // 2, RAW), 1, q_gu[:, f, RAW // 2:RAW])]
                    else:
                        parts = [(slice(k, k + D), 2, q_dn[:, 2 * f + k // D, :]) for k in range(0, down_width(f), D)]
                    for cols, w, _ in parts:
                        link(nc.vector.tensor_scalar(qtmp[:, cols], raw[:, n % RAW_SLOTS, cols],
                                                     scl[:, 9 + w:10 + w], None, ALU.is_lt))
                    for i, (cols, w, to) in enumerate(parts):
                        last = nc.vector.scalar_tensor_tensor(
                            out=to, in0=raw[:, n % RAW_SLOTS, cols], scalar=scl[:, 6 + w:7 + w], in1=qtmp[:, cols],
                            op0=ALU.is_gt, op1=ALU.subtract)
                        if i < len(parts) - 1:
                            link(last)
                    last.then_inc(tern_ready, 1)
                elif kind == "ln1":
                    t = at[0]
                    job = ("down", t // NC, t % NC)
                    v.wait_ge(b_done, JOB_B[job] + 1)
                    v.wait_ge(u_ready, t + 1)
                    nc.vector.tensor_tensor(x[:, t, :], bank_b(job), x[:, t, :], ALU.add).then_inc(freed_b(job)[0], 1)
                    v.wait_ge(*freed_b(job))
                    statistics(t, t)
                elif kind == "ln1x":
                    t = at[0]
                    i = norm_number(("ln1", t))
                    v.wait_ge(rstd_ready, i + 1)
                    nc.vector.tensor_scalar(x[:, t, :], x[:, t, :], mv[:, t, 0:1], rstd[:, i:i + 1], ALU.subtract,
                                            ALU.mult).then_inc(ln1_ready, 1)
                elif kind == "ffn":
                    b, f = at
                    n = FF * b + f
                    v.wait_ge(*freed_a(("fg", b, f)))
                    job = ("fu", b, f)
                    v.wait_ge(a_done, JOB_A[job] + 1)
                    if n >= 2:
                        v.wait_ge(int_ready, n - 1)
                    nc.vector.tensor_tensor(prod_t[:, n % 2, :], gate_t[:, n % 2, :], bank_a(job), ALU.mult)\
                        .then_inc(freed_a(job)[0], 1)
                elif kind == "ffndown":
                    t = tile_of(step)
                    v.wait_ge(b_done, JOB_B[step] + 1)
                    v.wait_ge(ln1_ready, t + 1)
                    nc.vector.scalar_tensor_tensor(out=x[:, t, :], in0=bank_b(step), scalar=scl[:, 13:14],
                                                   in1=x[:, t, :], op0=ALU.mult, op1=ALU.add)\
                        .then_inc(freed_b(step)[0], 1)
                    v.wait_ge(*freed_b(step))
                    statistics(t, NT + t)
                elif kind == "ln2":
                    t = tile_of(step)
                    i = norm_number(step)
                    v.wait_ge(rstd_ready, i + 1)
                    nc.vector.tensor_scalar(x[:, t, :], x[:, t, :], mv[:, NT + t, 0:1], rstd[:, i:i + 1],
                                            ALU.subtract, ALU.mult).then_inc(out_ready, 1)

        @block.tensor
        def _(pe):
            def open_a(job):
                if JOB_A[job] >= 4:
                    pe.wait_ge(a_free[JOB_A[job] % 4], JOB_A[job] // 4)
                return bank_a(job)

            def open_b(job):
                if JOB_B[job] >= 4:
                    pe.wait_ge(b_free[JOB_B[job] % 4], JOB_B[job] // 4)
                return bank_b(job)

            def split_product(ps, parts, first=True, last=True):
                for i, (sh, sl, mh, ml) in enumerate(parts):
                    nc.tensor.matmul(ps, sh, mh, start=first and i == 0, stop=False)
                    nc.tensor.matmul(ps, sh, ml, start=False, stop=False)
                    done = nc.tensor.matmul(ps, sl, mh, start=False, stop=last and i == len(parts) - 1)
                return done

            def turn(step, tile):
                ps = open_b(step)
                for k in range(KD):
                    done = nc.tensor.transpose(ps[:, chunk(k)], tile[:, chunk(k)], ident[:])
                done.then_inc(b_done, 1)

            def seq(tile, k, b):
                return tile[:, k, b * L:(b + 1) * L]

            pe.wait_ge(consts_ready, 1)
            for step in SCHEDULE:
                kind, at = step[0], step[1:]
                if kind == "turn1":
                    pe.wait_ge(nrm_ready, at[0] + 1)
                    turn(step, nrm[:, at[0] % 2, :])
                elif kind == "turn2":
                    t = tile_of(step)
                    pe.wait_ge(nrm_ready, NT + t + 1)
                    turn(step, nrm[:, t % 2, :])
                elif kind == "ln1t":
                    pe.wait_ge(ln1_ready, at[0] + 1)
                    turn(step, x[:, at[0], :])
                elif kind == "dt":
                    b = at[0]
                    for c in range(NC):
                        pe.wait_ge(*freed_b(("turn1", NC * b + c)))
                    pe.wait_ge(wdt_ready, 2)
                    ps = open_a(("dt", b))
                    for c in range(NC):
                        t = NC * b + c
                        done = split_product(ps[:, H * c:H * c + H],
                                             [(xT_h[:, k, chunk(t)], xT_l[:, k, chunk(t)], wdt_h[:, H * k:H * k + H],
                                               wdt_l[:, H * k:H * k + H]) for k in range(KD)])
                    done.then_inc(a_done, 1)
                    pe.wait_ge(dt_ready, b + 1)
                    ps = open_b(("cs", b))
                    nc.tensor.matmul(ps[:, 0:NC * H], tri[:], dtw[:, 5, :], start=True, stop=True).then_inc(b_done, 1)
                elif kind == "inproj":
                    b, j = at
                    pe.wait_ge(low_ready, split_count("in", j // 2))
                    ps = open_a(("in", b, j))
                    cols = [slice(2 * P * k + P * (j % 2), 2 * P * k + P * (j % 2) + P) for k in range(KD)]
                    split_product(ps, [(win_h[:, j // 2, cols[k]], win_l[:, j // 2, cols[k]], seq(xT_h, k, b),
                                        seq(xT_l, k, b)) for k in range(KD)]).then_inc(a_done, 1)
                elif kind == "chunk":
                    b, c = at
                    pe.wait_ge(xbc_ready, NX * (b + 1))
                    ps = open_b(("xb", b, c))
                    nc.tensor.transpose(ps[:, 0:P], xbc[b][:, 0, chunk(c)], ident[:])
                    nc.tensor.transpose(ps[:, P:2 * P], xbc[b][:, 1, chunk(c)], ident[:]).then_inc(b_done, 1)
                    pe.wait_ge(*freed_b(("cs", b)))
                    ps = open_b(("csb", b, c))
                    for h in range(H):
                        done = nc.tensor.matmul(ps[:, chunk(h)],
                                                csT[:, b, H * c + h:H * c + h + 1].to_broadcast([P, P]), ident[:],
                                                start=True, stop=True)
                    done.then_inc(b_done, 1)
                    ps = open_b(("cb", b, c))
                    nc.tensor.matmul(heads(ps), xbc[b][:, 1, chunk(c)], xbc[b][:, 2:NX, chunk(c)], start=True,
                                     stop=True).then_inc(b_done, 1)
                elif kind == "state":
                    b, c = at
                    t = NC * b + c
                    pe.wait_ge(*freed_b(("xb", b, c)))
                    if c < NC - 1:
                        pe.wait_ge(xs_ready, (NC - 1) * b + c + 1)
                        ps = open_b(("st", b, c))
                        nc.tensor.matmul(ps, xnbn[:, t % 2, P:2 * P], xs[:], start=True, stop=True).then_inc(b_done, 1)
                    ps = open_b(("y", b, c))
                    pe.wait_ge(diag_ready, 1)
                    nc.tensor.matmul(ps, xnbn[:, t % 2, 0:P], diag_d[:], start=True, stop=False)
                    if c > 0:
                        pe.wait_ge(*freed_b(("st", b, c - 1)))
                        pe.wait_ge(cs_scaled, (NC - 1) * b + c)
                        for h in range(H):
                            nc.tensor.matmul(ps[:, chunk(h)], state[:, (c - 1) % 2, chunk(h)],
                                             ecs[:, t % 2, chunk(h)], start=False, stop=False)
                    pe.wait_ge(*freed_b(("cb", b, c)))
                    done = nc.tensor.matmul(ps, xnbn[:, t % 2, 0:P], decay[:, t % 2, :], start=False, stop=True)
                    done.then_inc(b_done, 1)
                elif kind == "outproj":
                    t = tile_of(step)
                    pe.wait_ge(y_ready, t + 1)
                    pe.wait_ge(low_ready, split_count("out", 1))
                    ps = open_b(step)
                    w = [slice(D * (h % 2), D * (h % 2) + D) for h in range(H)]
                    split_product(ps, [(yt_h[:, chunk(h)], yt_l[:, chunk(h)], wout_h[:, h // 2, w[h]],
                                        wout_l[:, h // 2, w[h]]) for h in range(H)]).then_inc(b_done, 1)
                elif kind == "gateup":
                    b, f = at
                    pe.wait_ge(low_ready, split_count("gu", b, f))
                    for c in range(NC):
                        pe.wait_ge(*freed_b(("turn2", b, c)))
                    slot = wst_slot("gu", b, f)
                    for half, job in enumerate((("g", b, f), ("u", b, f))):
                        ps = open_a(job)
                        cols = [slice((half * KD + k) * P, (half * KD + k + 1) * P) for k in range(KD)]
                        done = split_product(ps, [(wst[:, slot, 0, cols[k]], wst[:, slot, 1, cols[k]],
                                                   seq(xT_h, k, b), seq(xT_l, k, b)) for k in range(KD)])
                        done.then_inc(a_done, 1)
                elif kind == "down":
                    b, f = at
                    n = FM * b + f
                    pe.wait_ge(low_ready, split_count("dn", b, f // 2))
                    pe.wait_ge(actl_ready, n + 1)
                    slot = wst_slot("dn", b, f // 2)
                    cols = slice(D * (f % 2), D * (f % 2) + D)
                    for c in range(NC):
                        job = ("down", b, c)
                        ps = open_b(job) if f == 0 else bank_b(job)
                        done = split_product(ps, [(act_hl[:, n % 3, 0, chunk(c)], act_hl[:, n % 3, 1, chunk(c)],
                                                   wst[:, slot, 0, cols], wst[:, slot, 1, cols])],
                                             first=f == 0, last=f == FM - 1)
                        if f == FM - 1:
                            done.then_inc(b_done, 1)
                        elif c == NC - 1:
                            done.then_inc(act_free, 1)
                elif kind == "scales":
                    pe.wait_ge(*raw_used(SUMS[-1]))
                    ps = open_b(step)
                    nc.tensor.matmul(ps[:, 0:3 * FF], ones[:], absum[:, 0:3 * FF], start=True, stop=True)\
                        .then_inc(b_done, 1)
                elif kind == "ffn":
                    b, f = at
                    pe.wait_ge(tern_ready, [LOADS[n] for n in TERN].index(("qgu", f)) + 1)
                    for c in range(NC):
                        pe.wait_ge(*freed_b(("ln1t", NC * b + c)))
                    for half, job in enumerate((("fg", b, f), ("fu", b, f))):
                        ps = open_a(job)
                        for k in range(KD):
                            w = q_gu[:, f, (half * KD + k) * P:(half * KD + k + 1) * P]
                            nc.tensor.matmul(ps, w, seq(xT_h, k, b), start=k == 0, stop=False)
                            done = nc.tensor.matmul(ps, w, seq(xT_l, k, b), start=False, stop=k == KD - 1)
                        done.then_inc(a_done, 1)
                elif kind == "ffndown":
                    b, c = at
                    ps = open_b(step)
                    pe.wait_ge(tern_ready, len(TERN))
                    for f in range(FF):
                        pe.wait_ge(int_ready, FF * b + f + 1)
                        nc.tensor.matmul(ps, int_h[:, f, chunk(c)], q_dn[:, f, :], start=f == 0, stop=False)
                        done = nc.tensor.matmul(ps, int_l[:, f, chunk(c)], q_dn[:, f, :], start=False,
                                                stop=f == FF - 1)
                    done.then_inc(b_done, 1)


def _columns(w, per):
    n_out, n_in = w.shape
    a = w.reshape(n_out // (per * P), per * P, n_in // P, P)
    return np.ascontiguousarray(a.transpose(0, 3, 2, 1)).reshape(n_out // (per * P), P, -1)


def _gate_up(gate, up):
    return np.ascontiguousarray(np.concatenate([_columns(gate, 1), _columns(up, 1)], axis=2))


def _down(w):
    n_out, n_in = w.shape
    a = w.T.reshape(n_in // (2 * P), 2, P, n_out)
    return np.ascontiguousarray(a.transpose(0, 2, 1, 3)).reshape(n_in // (2 * P), P, 2 * n_out)


def kernel(**inputs):
    import concourse.bacc as bacc
    from concourse.bass_utils import run_bass_kernel_spmd

    a = {k.replace("L0_attn_", "").replace("L0_ffn_", "ffn_"): np.asarray(v) for k, v in inputs.items()}
    w_in = a["w_in"]
    order = np.concatenate([w_in[D:D + NX * P], w_in[0:D]])
    w_dt = w_in[D + NX * P:].T.reshape(KD, P, H).transpose(1, 0, 2).reshape(P, KD * H)

    def padded(w, axis, tiles):
        pad = [(0, 0), (0, 0)]
        pad[axis] = (0, tiles * P - w.shape[axis])
        return np.pad(w, pad)

    arrays = {
        "hidden": a["hidden_states"].reshape(NT, P, D),
        "w_in_t": _columns(order, 2),
        "w_dt": np.ascontiguousarray(w_dt),
        "conv_w": np.ascontiguousarray(a["conv_w"].reshape(NX, P, TAPS).transpose(1, 0, 2)),
        "conv_b": np.ascontiguousarray(a["conv_b"].reshape(NX, P).T),
        "a_log": a["A_log"].reshape(1, H),
        "d_skip": a["D"].reshape(1, H),
        "dt_bias": a["dt_bias"].reshape(1, H),
        "w_out_t": _down(a["w_out"]),
        "ln1_w": a["ln1_w"].reshape(1, D),
        "ln2_w": a["ln2_w"].reshape(1, D),
        "w_gu_t": _gate_up(a["gate_w"], a["up_w"]),
        "w_dn_t": _down(a["down_w"]),
        "f_gu_t": _gate_up(padded(a["ffn_w_gate"], 0, FF), padded(a["ffn_w_up"], 0, FF)),
        "f_dn_t": _down(padded(a["ffn_w_down"], 1, FF + FF % 2)),
    }
    arrays = {k: np.ascontiguousarray(v) for k, v in arrays.items()}
    nc = bacc.Bacc("TRN2", target_bir_lowering=False, num_devices=1)
    args = [nc.dram_tensor(f"in_{k}", v.shape, mybir.dt.from_np(v.dtype), kind="ExternalInput").ap()
            for k, v in arrays.items()]
    out = nc.dram_tensor("out", (NT, P, D), F32, kind="ExternalOutput").ap()
    layer_kernel(nc, *args, out)
    r = run_bass_kernel_spmd(nc, [{f"in_{k}": v for k, v in arrays.items()}], core_ids=[0])
    return r.results[0]["out"].reshape(NB, L, D)
```
